# Optimizing a Trainium2 kernel written in Bass

```python
import numpy as np
import jax
import jax.numpy as jnp

def _softmax(x, axis=-1):
    return jax.nn.softmax(x, axis=axis)

def _gelu(x):
    return jax.nn.gelu(x, approximate=True)

def _silu(x):
    return jax.nn.silu(x)

def _sigmoid(x):
    return jax.nn.sigmoid(x)

def _layernorm(x, axis=-1, eps=1e-05):
    m = jnp.mean(x, axis=axis, keepdims=True)
    v = jnp.var(x, axis=axis, keepdims=True)
    return (x - m) / jnp.sqrt(v + eps)

def _scatter_add(tgt, idx, src, axis=0):
    return tgt.at[idx].add(src)

def _segment_sum(src, seg, n):
    return jax.ops.segment_sum(src, seg, n)
kernel_name = 'mk_dlrm_tower_d1_rec_r8_c86f00'

def setup_inputs(seed: int=0):
    np.random.seed(seed)
    _w = jnp.asarray

    def _rec_inputs():
        import jax
        import jax.numpy as jnp
        _tk = jax.random.key(seed)
        ids = jnp.stack([jax.random.randint(jax.random.fold_in(_tk, 200 + f), (2048,), 0, v, jnp.int32) for f, v in enumerate([1250, 125000, 1000, 1000, 1250, 12500, 1000, 12500, 1000, 1000, 1000, 12500, 1000, 1250, 1000, 1000, 12500, 12500, 12500, 1250, 1250, 12500, 1250, 12500, 1000, 1000])], axis=1)
        tbl_0 = 0.05 * jax.random.normal(jax.random.fold_in(_tk, 500 + 0), (1250, 128), jnp.float32)
        tbl_1 = 0.05 * jax.random.normal(jax.random.fold_in(_tk, 500 + 1), (125000, 128), jnp.float32)
        tbl_2 = 0.05 * jax.random.normal(jax.random.fold_in(_tk, 500 + 2), (1000, 128), jnp.float32)
        tbl_3 = 0.05 * jax.random.normal(jax.random.fold_in(_tk, 500 + 3), (1000, 128), jnp.float32)
        tbl_4 = 0.05 * jax.random.normal(jax.random.fold_in(_tk, 500 + 4), (1250, 128), jnp.float32)
        tbl_5 = 0.05 * jax.random.normal(jax.random.fold_in(_tk, 500 + 5), (12500, 128), jnp.float32)
        tbl_6 = 0.05 * jax.random.normal(jax.random.fold_in(_tk, 500 + 6), (1000, 128), jnp.float32)
        tbl_7 = 0.05 * jax.random.normal(jax.random.fold_in(_tk, 500 + 7), (12500, 128), jnp.float32)
        tbl_8 = 0.05 * jax.random.normal(jax.random.fold_in(_tk, 500 + 8), (1000, 128), jnp.float32)
        tbl_9 = 0.05 * jax.random.normal(jax.random.fold_in(_tk, 500 + 9), (1000, 128), jnp.float32)
        tbl_10 = 0.05 * jax.random.normal(jax.random.fold_in(_tk, 500 + 10), (1000, 128), jnp.float32)
        tbl_11 = 0.05 * jax.random.normal(jax.random.fold_in(_tk, 500 + 11), (12500, 128), jnp.float32)
        tbl_12 = 0.05 * jax.random.normal(jax.random.fold_in(_tk, 500 + 12), (1000, 128), jnp.float32)
        tbl_13 = 0.05 * jax.random.normal(jax.random.fold_in(_tk, 500 + 13), (1250, 128), jnp.float32)
        tbl_14 = 0.05 * jax.random.normal(jax.random.fold_in(_tk, 500 + 14), (1000, 128), jnp.float32)
        tbl_15 = 0.05 * jax.random.normal(jax.random.fold_in(_tk, 500 + 15), (1000, 128), jnp.float32)
        tbl_16 = 0.05 * jax.random.normal(jax.random.fold_in(_tk, 500 + 16), (12500, 128), jnp.float32)
        tbl_17 = 0.05 * jax.random.normal(jax.random.fold_in(_tk, 500 + 17), (12500, 128), jnp.float32)
        tbl_18 = 0.05 * jax.random.normal(jax.random.fold_in(_tk, 500 + 18), (12500, 128), jnp.float32)
        tbl_19 = 0.05 * jax.random.normal(jax.random.fold_in(_tk, 500 + 19), (1250, 128), jnp.float32)
        tbl_20 = 0.05 * jax.random.normal(jax.random.fold_in(_tk, 500 + 20), (1250, 128), jnp.float32)
        tbl_21 = 0.05 * jax.random.normal(jax.random.fold_in(_tk, 500 + 21), (12500, 128), jnp.float32)
        tbl_22 = 0.05 * jax.random.normal(jax.random.fold_in(_tk, 500 + 22), (1250, 128), jnp.float32)
        tbl_23 = 0.05 * jax.random.normal(jax.random.fold_in(_tk, 500 + 23), (12500, 128), jnp.float32)
        tbl_24 = 0.05 * jax.random.normal(jax.random.fold_in(_tk, 500 + 24), (1000, 128), jnp.float32)
        tbl_25 = 0.05 * jax.random.normal(jax.random.fold_in(_tk, 500 + 25), (1000, 128), jnp.float32)
        _rk = jax.random.fold_in(_tk, 7)
        r_dense_features = -0.000292821 + 1.00034 * jax.random.normal(jax.random.fold_in(_rk, 101), (2048, 128), jnp.float32)
        W_top1 = 0.0405887 * jax.random.normal(jax.random.fold_in(_tk, 801), (607, 512), jnp.float32)
        W_top2 = 0.0441942 * jax.random.normal(jax.random.fold_in(_tk, 802), (512, 256), jnp.float32)
        W_top3 = 0.0625 * jax.random.normal(jax.random.fold_in(_tk, 803), (256, 1), jnp.float32)
        b_top1 = jnp.zeros((512,), jnp.float32)
        b_top2 = jnp.zeros((256,), jnp.float32)
        return (r_dense_features, ids, tbl_0, tbl_1, tbl_2, tbl_3, tbl_4, tbl_5, tbl_6, tbl_7, tbl_8, tbl_9, tbl_10, tbl_11, tbl_12, tbl_13, tbl_14, tbl_15, tbl_16, tbl_17, tbl_18, tbl_19, tbl_20, tbl_21, tbl_22, tbl_23, tbl_24, tbl_25, W_top1, b_top1, W_top2, b_top2, W_top3)
    r_dense_features, ids, tbl_0, tbl_1, tbl_2, tbl_3, tbl_4, tbl_5, tbl_6, tbl_7, tbl_8, tbl_9, tbl_10, tbl_11, tbl_12, tbl_13, tbl_14, tbl_15, tbl_16, tbl_17, tbl_18, tbl_19, tbl_20, tbl_21, tbl_22, tbl_23, tbl_24, tbl_25, W_top1, b_top1, W_top2, b_top2, W_top3 = _rec_inputs()

    def _L0_rec_setup():
        import jax, jax.numpy as jnp
        import numpy as np
        F = 26
        _TRIU_I, _TRIU_J = np.triu_indices(F + 1, k=1)
        key = jax.random.key(seed)
        k1, k2 = jax.random.split(key)
        B, D = (4096, 128)
        dense_features = jax.random.normal(k1, (B, D), dtype=jnp.float32)
        sparse_features = jax.random.normal(k2, (B, F, D), dtype=jnp.float32)
        return {'dense_features': dense_features, 'sparse_features': sparse_features}
    _L0_rec_all = _L0_rec_setup()
    _L0_rec_in = {k: v for k, v in _L0_rec_all.items() if k in ()}
    del _L0_rec_all
    return {'r_dense_features': r_dense_features, 'ids': ids, 'tbl_0': tbl_0, 'tbl_1': tbl_1, 'tbl_2': tbl_2, 'tbl_3': tbl_3, 'tbl_4': tbl_4, 'tbl_5': tbl_5, 'tbl_6': tbl_6, 'tbl_7': tbl_7, 'tbl_8': tbl_8, 'tbl_9': tbl_9, 'tbl_10': tbl_10, 'tbl_11': tbl_11, 'tbl_12': tbl_12, 'tbl_13': tbl_13, 'tbl_14': tbl_14, 'tbl_15': tbl_15, 'tbl_16': tbl_16, 'tbl_17': tbl_17, 'tbl_18': tbl_18, 'tbl_19': tbl_19, 'tbl_20': tbl_20, 'tbl_21': tbl_21, 'tbl_22': tbl_22, 'tbl_23': tbl_23, 'tbl_24': tbl_24, 'tbl_25': tbl_25, 'W_top1': W_top1, 'b_top1': b_top1, 'W_top2': W_top2, 'b_top2': b_top2, 'W_top3': W_top3}

def reference(r_dense_features, ids, tbl_0, tbl_1, tbl_2, tbl_3, tbl_4, tbl_5, tbl_6, tbl_7, tbl_8, tbl_9, tbl_10, tbl_11, tbl_12, tbl_13, tbl_14, tbl_15, tbl_16, tbl_17, tbl_18, tbl_19, tbl_20, tbl_21, tbl_22, tbl_23, tbl_24, tbl_25, W_top1, b_top1, W_top2, b_top2, W_top3):
    import jax
    import jax.numpy as jnp

    def _L0_rec_ref(dense_features, sparse_features):
        import jax, jax.numpy as jnp
        import numpy as np
        F = 26
        _TRIU_I, _TRIU_J = np.triu_indices(F + 1, k=1)
        combined = jnp.concatenate([dense_features[:, None, :], sparse_features], axis=1)
        interactions = jnp.einsum('bfd,bgd->bfg', combined, combined)
        interactions_flat = interactions[:, _TRIU_I, _TRIU_J]
        return jnp.concatenate([dense_features, interactions_flat], axis=1)
    e = jnp.stack([tbl_0[ids[:, 0]], tbl_1[ids[:, 1]], tbl_2[ids[:, 2]], tbl_3[ids[:, 3]], tbl_4[ids[:, 4]], tbl_5[ids[:, 5]], tbl_6[ids[:, 6]], tbl_7[ids[:, 7]], tbl_8[ids[:, 8]], tbl_9[ids[:, 9]], tbl_10[ids[:, 10]], tbl_11[ids[:, 11]], tbl_12[ids[:, 12]], tbl_13[ids[:, 13]], tbl_14[ids[:, 14]], tbl_15[ids[:, 15]], tbl_16[ids[:, 16]], tbl_17[ids[:, 17]], tbl_18[ids[:, 18]], tbl_19[ids[:, 19]], tbl_20[ids[:, 20]], tbl_21[ids[:, 21]], tbl_22[ids[:, 22]], tbl_23[ids[:, 23]], tbl_24[ids[:, 24]], tbl_25[ids[:, 25]]], axis=1)
    z = _L0_rec_ref(r_dense_features, e)
    z = z.reshape(z.shape[0], -1)
    h = jnp.concatenate([z, r_dense_features], axis=1)
    h = jnp.maximum(h @ W_top1 + b_top1, 0.0)
    h = jnp.maximum(h @ W_top2 + b_top2, 0.0)
    y = h @ W_top3
    return y

_drawn_inputs = setup_inputs


def setup_inputs(seed=0):
    import zlib

    import numpy as np

    out = dict(_drawn_inputs(seed))
    spreads = {'b_top1': (0.0, 0.1), 'b_top2': (0.0, 0.1)}
    factors = {}
    for name, (base, spread) in spreads.items():
        noise = np.random.default_rng([zlib.crc32(name.encode()), seed]).standard_normal(out[name].shape)
        drawn = base * np.exp(spread * noise) if base else spread * noise
        out[name] = jnp.asarray(drawn.astype(out[name].dtype))
    for name, factor in factors.items():
        out[name] = (out[name] * factor).astype(out[name].dtype)
    return out
```

```python
from contextlib import ExitStack

import concourse.bass as bass
from concourse import mybir

F32 = mybir.dt.float32
I32 = mybir.dt.int32
ACT = mybir.ActivationFunctionType
ALU = mybir.AluOpType

P = 128


def dlrm_tower(nc, dense, ids, tables, w1, b1, w2, b2, w3, out):
    batch, d_emb = dense.shape
    n_tab = len(tables)
    NF = n_tab + 1
    NP = NF * (NF - 1) // 2
    TILES = batch // P
    TPB = 4
    BLOCKS = TILES // TPB
    COLS = TPB * P
    J = 4
    U = P // J
    H1, H2 = w2.shape
    C1, C2 = H1 // P, H2 // P
    ZC = 3
    ZK = NP // ZC
    assert d_emb == P and ZK * ZC == NP and w1.shape[0] == 2 * P + NP

    TQ = 4
    T_FILLS = -(-NF // TQ)
    GQ = 4
    G_FILLS = U // GQ
    A_UNITS = -(-(NF - 1) // TQ)
    UNITS = [("rows", i) for i in range(A_UNITS)] + [("pairs", i) for i in range(ZC)] \
        + [("layer1", i) for i in range(C1)] + [("layer2", i) for i in range(C2)] + [("layer3", 0)]
    NU = len(UNITS)
    ROWS_DONE, PAIRS_DONE, L1_DONE, L2_DONE = A_UNITS, A_UNITS + ZC, A_UNITS + ZC + C1, NU - 1
    UNIT_ENGINE = ["V" if k == "rows" else "V" if k == "pairs" else "S" for k, _ in UNITS]

    def emptied_by(engine, n):
        return sum(e == engine for e in UNIT_ENGINE[:n])

    def steps():
        plan = []
        later = list(range(A_UNITS, NU))
        for t in range(TPB):
            for k in range(G_FILLS):
                if k < T_FILLS:
                    plan.append(("T", t, k))
                if t == 1 and k < A_UNITS:
                    plan.append(("W", 0, k))
                if t != 1:
                    plan.append(("G", t - 1, k))
                if t == 2 and k % 2 == 1 or t == 3 and k % 2 == 1:
                    if later:
                        plan.append(("W", 0, later.pop(0)))
            if t == 1:
                for k in range(G_FILLS):
                    plan.append(("G", 0, k))
                    if k % 3 == 2:
                        plan.append(("W", 0, later.pop(0)))
        plan += [("W", 0, n) for n in later]
        return plan

    BODY = steps()
    FIRST = [s for s in BODY if s[0] == "T" or s[0] == "G" and s[1] >= 0]
    LAST = [("G", -1, k) for k in range(G_FILLS)] + [("W", 0, n) for n in range(NU)]

    with ExitStack() as ctx:
        def sb(name, shape, dt=F32):
            return ctx.enter_context(nc.sbuf_tensor(name, shape, dt))

        def bank(name):
            return ctx.enter_context(nc.psum_tensor(name, [P, 512], F32))

        def sem(name):
            return ctx.enter_context(nc.semaphore(name))

        idx = sb("idx", [P, TPB, n_tab], I32)
        rows = sb("rows", [P, TPB, NF, P])
        emb_t = sb("emb_t", [P, TPB, P, 32])
        dense_t = sb("dense_t", [P, BLOCKS * COLS])
        gram = sb("gram", [P, TPB * U, NF])
        pair_rows = sb("pair_rows", [P, J, NP])
        pair_cols = sb("pair_cols", [ZK, ZC, COLS])
        h1 = sb("h1", [P, C1, COLS])
        h2 = sb("h2", [P, C2, COLS])
        w1z = sb("w1z", [ZK, ZC, H1])
        w1a = sb("w1a", [P, H1])
        w1b = sb("w1b", [P, H1])
        w1d = sb("w1d", [P, H1])
        w2s = sb("w2s", [P, C1, H2])
        w3s = sb("w3s", [P, C2])
        b1s = sb("b1s", [P, C1])
        b2s = sb("b2s", [P, C2])
        y = sb("y", [1, batch])
        ident = sb("ident", [P, P])

        t_bank = [bank(f"t_bank{i}") for i in range(2)]
        g_bank = [bank(f"g_bank{i}") for i in range(2)]
        w_bank = [bank(f"w_bank{i}") for i in range(4)]

        idx_loaded = [sem(f"idx_loaded{t}") for t in range(TPB)]
        dense_loaded = [sem(f"dense_loaded{t}") for t in range(TPB)]
        gathered = [[sem(f"gathered{t}_{k}") for k in range(T_FILLS)] for t in range(TPB)]
        rows_free = sem("rows_free")
        weights_loaded = sem("weights_loaded")
        ident_zeroed = sem("ident_zeroed")
        ident_ready = sem("ident_ready")
        pad_zeroed = sem("pad_zeroed")
        w1d_ready = sem("w1d_ready")
        transposed = sem("transposed")
        emb_by_v = sem("emb_by_v")
        emb_by_s = sem("emb_by_s")
        dense_t_ready = sem("dense_t_ready")
        multiplied = sem("multiplied")
        gram_by_v = sem("gram_by_v")
        gram_by_s = sem("gram_by_s")
        unit_filled = sem("unit_filled")
        unit_by_v = sem("unit_by_v")
        unit_by_s = sem("unit_by_s")
        stored = sem("stored")

        NT = TPB * T_FILLS
        NG = TPB * G_FILLS
        assert NT % 4 == 0 and NG % 2 == 0
        N_WEIGHTS = 7

        dense_tiles = dense.rearrange("(p n) d -> p n d", n=TILES)
        ids_tiles = ids.rearrange("(p n) f -> p n f", n=TILES)
        out_row = out.rearrange("b one -> one b")

        def fill_features(k):
            return list(range(TQ * k, min(TQ * k + TQ, NF)))

        def gathers(k):
            return len([f for f in fill_features(k) if f > 0])

        def blocks(eng, body):
            body(0, FIRST)
            with eng.Fori(1, BLOCKS) as b:
                body(b, BODY)
            body(BLOCKS, LAST)

        block = ctx.enter_context(nc.Block())

        @block.sync
        def _(sp):
            def load_tile(b, t):
                sp.dma_start(idx[:, t, :], ids_tiles[:, bass.ds(b * TPB + t, 1), :].rearrange("p n f -> p (n f)")
                             ).then_inc(idx_loaded[t], 16)
                sp.dma_start(rows[:, t, 0, :], dense_tiles[:, bass.ds(b * TPB + t, 1), :].rearrange("p n d -> p (n d)")
                             ).then_inc(dense_loaded[t], 16)

            for t in range(TPB):
                load_tile(0, t)
            for dst, src in (
                (w1z[:], w1[P:P + NP, :].rearrange("(c p) n -> p c n", p=ZK)),
                (w1a[:], w1[0:P, :]), (w1b[:], w1[P + NP:, :]),
                (w2s[:], w2.rearrange("(p c) n -> p c n", c=C1)),
                (w3s[:], w3.rearrange("(p c) one -> p (c one)", c=C2)),
                (b1s[:], b1.rearrange("(p c) -> p c", c=C1)),
                (b2s[:], b2.rearrange("(p c) -> p c", c=C2)),
            ):
                sp.dma_start(dst, src).then_inc(weights_loaded, 16)
            with sp.Fori(1, BLOCKS) as b:
                for t in range(TPB):
                    sp.wait_ge(transposed, NT * (b - 1) + T_FILLS * (t + 1))
                    load_tile(b, t)
            sp.wait_ge(unit_by_s, BLOCKS * emptied_by("S", NU) + 1)
            sp.dma_start(out_row, y[:]).then_inc(stored, 16)
            sp.wait_ge(stored, 16)

        @block.gpsimd
        def _(pool):
            nc.gpsimd.memset(ident[:], 0.0).then_inc(ident_zeroed, 1)
            pool.wait_ge(ident_zeroed, 1)
            nc.gpsimd.affine_select(out=ident[:], in_=ident[:], compare_op=ALU.not_equal, fill=1.0,
                                    base=0, pattern=[[-1, P]], channel_multiplier=1).then_inc(ident_ready, 1)

            def gather_block(b, again):
                for t in range(TPB):
                    pool.wait_ge(idx_loaded[t], 16 * (b + 1))
                    for k in range(T_FILLS):
                        if again:
                            pool.wait_ge(transposed, NT * (b - 1) + T_FILLS * t + k + 1)
                            pool.sem_inc(rows_free, 1)
                        for f in fill_features(k):
                            if f > 0:
                                nc.gpsimd.indirect_dma_start(
                                    rows[:, t, f, :], None, tables[f - 1],
                                    bass.IndirectOffsetOnAxis(ap=idx[:, t, f - 1:f], axis=0),
                                ).then_inc(gathered[t][k], 16)

            gather_block(0, False)
            with pool.Fori(1, BLOCKS) as b:
                gather_block(b, True)

        @block.tensor
        def _(pe):
            def transposes(b, t, k):
                n = T_FILLS * t + k
                if k == 0:
                    pe.wait_ge(dense_loaded[t], 16 * (b + 1))
                pe.wait_ge(gathered[t][k], 16 * gathers(k) * (b + 1))
                if n % 2 == 0:
                    if n >= 2 or not first:
                        pe.wait_ge(emb_by_v, NT // 2 * b + n // 2)
                elif n >= 3 or not first:
                    pe.wait_ge(emb_by_s, NT // 2 * b + n // 2)
                for i, f in enumerate(fill_features(k)):
                    last = nc.tensor.transpose(t_bank[n % 2][:, i * P:(i + 1) * P], rows[:, t, f, :], ident[:])
                last.then_inc(transposed, 1)

            def products(b, t, k):
                m = G_FILLS * t + k
                if k == 0:
                    n = T_FILLS * (t + 1)
                    pe.wait_ge(emb_by_v, NT // 2 * b + (n + 1) // 2)
                    pe.wait_ge(emb_by_s, NT // 2 * b + n // 2)
                if not (first and m < 2):
                    pe.wait_ge(gram_by_v, NG * b + m - 1)
                    pe.wait_ge(gram_by_s, NG * b + m - 1)
                for i in range(GQ):
                    group = emb_t[:, t % TPB, J * (GQ * k + i):J * (GQ * k + i + 1), :]
                    last = nc.tensor.matmul(g_bank[m % 2][:, i * J * NF:(i + 1) * J * NF],
                                            group.rearrange("p j f -> p (j f)"), group[:, :, 0:NF],
                                            start=True, stop=True)
                last.then_inc(multiplied, 1)

            def unit(b, n):
                kind, i = UNITS[n]
                to = w_bank[n % 4]
                done = b - 1
                if n == 0:
                    pe.wait_ge(unit_by_s, emptied_by("S", NU) * done + 1)
                if n >= 4:
                    if UNIT_ENGINE[n - 4] == "V":
                        pe.wait_ge(unit_by_v, emptied_by("V", NU) * done + emptied_by("V", n - 3))
                    else:
                        pe.wait_ge(unit_by_s, emptied_by("S", NU) * done + emptied_by("S", n - 3) + 1)
                if kind == "rows":
                    if i == 0:
                        pe.wait_ge(gram_by_v, NG * b)
                        pe.wait_ge(gram_by_s, NG * b)
                    for q, a in enumerate(range(TQ * i, min(TQ * i + TQ, NF - 1))):
                        last = nc.tensor.transpose(to[:, q * P:(q + 1) * P], gram[:, :, a], ident[:])
                elif kind == "pairs":
                    if i == 0:
                        pe.wait_ge(unit_by_v, emptied_by("V", NU) * done + emptied_by("V", ROWS_DONE))
                    for j in range(J):
                        last = nc.tensor.transpose(to[0:ZK, j * P:(j + 1) * P],
                                                   pair_rows[:, j, i * ZK:(i + 1) * ZK], ident[:])
                elif kind == "layer1":
                    if i == 0:
                        pe.wait_ge(unit_by_v, emptied_by("V", NU) * done + emptied_by("V", PAIRS_DONE))
                        pe.wait_ge(dense_t_ready, TPB * b)
                    cols = slice(i, H1, C1)
                    nc.tensor.matmul(to[:], w1d[:, cols], dense_t[:, bass.ds(COLS * done, COLS)], start=True, stop=False)
                    for c in range(ZC):
                        last = nc.tensor.matmul(to[:], w1z[:, c, cols], pair_cols[:, c, :],
                                                start=False, stop=(c == ZC - 1))
                elif kind == "layer2":
                    if i == 0:
                        pe.wait_ge(unit_by_s, emptied_by("S", NU) * done + emptied_by("S", L1_DONE) + 1)
                    for c in range(C1):
                        last = nc.tensor.matmul(to[:], w2s[:, c, i:H2:C2], h1[:, c, :],
                                                start=(c == 0), stop=(c == C1 - 1))
                else:
                    pe.wait_ge(unit_by_s, emptied_by("S", NU) * done + emptied_by("S", L2_DONE) + 1)
                    for c in range(C2):
                        last = nc.tensor.matmul(to[0:1, :], w3s[:, c:c + 1], h2[:, c, :],
                                                start=(c == 0), stop=(c == C2 - 1))
                last.then_inc(unit_filled, 1)

            first = True

            def body(b, plan):
                nonlocal first
                first = plan is FIRST
                for kind, t, k in plan:
                    if kind == "T":
                        transposes(b, t, k)
                    elif kind == "G":
                        products(b, t, k)
                    else:
                        unit(b, k)

            pe.wait_ge(ident_ready, 1)
            pe.wait_ge(weights_loaded, 16 * N_WEIGHTS)
            pe.wait_ge(w1d_ready, 1)
            pe.wait_ge(pad_zeroed, 1)
            blocks(pe, body)

        def empty_tile_bank(eng, b, t, k):
            n = T_FILLS * t + k
            fs = fill_features(k)
            eng.wait_ge(transposed, NT * b + n + 1)
            src = t_bank[n % 2][:, 0:len(fs) * P].rearrange("p (f s) -> p s f", f=len(fs))
            return emb_t[:, t, :, fs[0]:fs[-1] + 1], src

        def gram_part(m, t, k, j):
            q = slice(32 * j, 32 * j + 32)
            src = g_bank[m % 2][:, 0:GQ * J * NF].rearrange("p (g j b) -> p g j b", g=GQ, j=J)
            s = U * (t % TPB) + GQ * k
            return gram[q, s:s + GQ, :], src[q, :, j, :]

        def unit_bank(eng, b, n):
            eng.wait_ge(unit_filled, NU * (b - 1) + n + 1)
            return w_bank[n % 4]

        @block.vector
        def _(dve):
            nc.vector.memset(emb_t[:, :, :, NF:], 0.0).then_inc(pad_zeroed, 1)
            dve.wait_ge(weights_loaded, 16 * N_WEIGHTS)
            nc.vector.tensor_tensor(w1d[:], w1a[:], w1b[:], ALU.add).then_inc(w1d_ready, 1)

            def body(b, plan):
                for kind, t, k in plan:
                    if kind == "T" and (T_FILLS * t + k) % 2 == 0:
                        dst, src = empty_tile_bank(dve, b, t, k)
                        nc.vector.tensor_copy(dst, src).then_inc(emb_by_v, 1)
                    elif kind == "G":
                        m = G_FILLS * t + k
                        dve.wait_ge(multiplied, NG * b + m + 1)
                        for j in (0, 1):
                            last = nc.vector.tensor_copy(*gram_part(m, t, k, j))
                        last.then_inc(gram_by_v, 1)
                    elif kind == "W" and UNIT_ENGINE[k] == "V":
                        work, i = UNITS[k]
                        src = unit_bank(dve, b, k)
                        if work == "rows":
                            for q, a in enumerate(range(TQ * i, min(TQ * i + TQ, NF - 1))):
                                at = a * NF - a * (a + 1) // 2
                                block_a = src[:, q * P:(q + 1) * P].rearrange("p (j b) -> p j b", j=J)
                                last = nc.vector.tensor_copy(pair_rows[:, :, at:at + NF - 1 - a],
                                                             block_a[:, :, a + 1:NF])
                        else:
                            last = nc.vector.tensor_copy(pair_cols[:, i, :], src[0:ZK, :])
                        last.then_inc(unit_by_v, 1)

            blocks(dve, body)

        @block.scalar
        def _(act):
            act.wait_ge(weights_loaded, 16 * N_WEIGHTS)
            nc.scalar.copy(y[:, 0:1], b1s[0:1, 0:1]).then_inc(unit_by_s, 1)

            def body(b, plan):
                for kind, t, k in plan:
                    if kind == "T":
                        n = T_FILLS * t + k
                        if n % 2 == 1:
                            dst, src = empty_tile_bank(act, b, t, k)
                            last = nc.scalar.copy(dst, src)
                            last.then_inc(emb_by_s, 1)
                        if k == 0:
                            for_t = emb_t[:, t, :, 0].rearrange("p (u j) -> p j u", j=J)
                            act.wait_ge(emb_by_v if n % 2 == 0 else emb_by_s, NT // 2 * b + n // 2 + 1)
                            cols = dense_t[:, bass.ds(COLS * b, COLS)].rearrange("p (j t u) -> p j t u", j=J, t=TPB)
                            nc.scalar.copy(cols[:, :, t, :], for_t).then_inc(dense_t_ready, 1)
                    elif kind == "G":
                        m = G_FILLS * t + k
                        act.wait_ge(multiplied, NG * b + m + 1)
                        for j in (2, 3):
                            last = nc.scalar.copy(*gram_part(m, t, k, j))
                        last.then_inc(gram_by_s, 1)
                    elif kind == "W" and UNIT_ENGINE[k] == "S":
                        work, i = UNITS[k]
                        src = unit_bank(act, b, k)
                        if work == "layer1":
                            last = nc.scalar.activation(h1[:, i, :], src[:], ACT.Relu, bias=b1s[:, i:i + 1])
                        elif work == "layer2":
                            last = nc.scalar.activation(h2[:, i, :], src[:], ACT.Relu, bias=b2s[:, i:i + 1])
                        else:
                            to = y[:, :].rearrange("o (u j n) -> o j n u", j=J, n=TILES)
                            last = nc.scalar.copy(to[:, :, bass.ds(TPB * (b - 1), TPB), :],
                                                  src[0:1, :].rearrange("o (j t u) -> o j t u", j=J, t=TPB))
                        last.then_inc(unit_by_s, 1)

            blocks(act, body)


N_TABLES = 26
_INS = ["r_dense_features", "ids"] + [f"tbl_{i}" for i in range(N_TABLES)] + ["W_top1", "b_top1", "W_top2", "b_top2", "W_top3"]


def kernel(**inputs):
    import numpy as _np
    import concourse.bacc as _bacc
    from concourse import mybir as _mybir
    from concourse.bass_utils import run_bass_kernel_spmd as _run

    nc = _bacc.Bacc("TRN2", target_bir_lowering=False, num_devices=1)
    arrays, aps = {}, {}
    for name in _INS:
        a = _np.ascontiguousarray(inputs[name])
        arrays[f"in_{name}"] = a
        aps[name] = nc.dram_tensor(f"in_{name}", a.shape, _mybir.dt.from_np(a.dtype), kind="ExternalInput").ap()
    batch = arrays["in_ids"].shape[0]
    out = nc.dram_tensor("out_y", (batch, 1), F32, kind="ExternalOutput").ap()
    dlrm_tower(nc, aps["r_dense_features"], aps["ids"], [aps[f"tbl_{i}"] for i in range(N_TABLES)],
               aps["W_top1"], aps["b_top1"], aps["W_top2"], aps["b_top2"], aps["W_top3"], out)
    r = _run(nc, [arrays], core_ids=[0])
    return r.results[0]["out_y"]
```

```python
from contextlib import ExitStack

import concourse.bass as bass
from concourse import mybir

F32 = mybir.dt.float32
F16 = mybir.dt.float16
BF16 = mybir.dt.bfloat16
I32 = mybir.dt.int32
ACT = mybir.ActivationFunctionType
ALU = mybir.AluOpType

P = 128
KEPT = (2, 3, 8, 9)
RESIDENT = KEPT + (10, 14, 24, 25)


def dlrm_tower(nc, dense, ids, ids_t, tables, w1, b1, w2, b2, w3, out):
    batch, d_emb = dense.shape
    n_tab = len(tables)
    NF = n_tab + 1
    NP = NF * (NF - 1) // 2
    TILES = batch // P
    TPB = 4
    BLOCKS = TILES // TPB
    COLS = TPB * P
    J = 4
    U = P // J
    GP = 32 * (J - 1) + NF
    H1, H2 = w2.shape
    C1, C2 = H1 // P, H2 // P
    ZC = 3
    ZK = NP // ZC
    assert d_emb == P and ZK * ZC == NP and w1.shape[0] == 2 * P + NP

    TQ = 4
    turned = [f for f in range(NF) if f - 1 not in KEPT]
    FILLS = []
    for f in turned:
        if FILLS and len(FILLS[-1]) < TQ and FILLS[-1][-1] == f - 1:
            FILLS[-1].append(f)
        else:
            FILLS.append([f])
    T_FILLS = len(FILLS)
    FIRST_FILLS = [[f for f in fs if f - 1 not in RESIDENT] for fs in FILLS]
    assert all(fs[-1] - fs[0] == len(fs) - 1 for fs in FIRST_FILLS)
    SLOT = {f: i for i, f in enumerate(turned)}
    GQ = 4
    G_FILLS = U // GQ

    NR, NK = len(RESIDENT), len(KEPT)
    V = tables[RESIDENT[0]].shape[0]
    V_C = -(-V // P)
    V_K = V // V_C
    HALVES = 2
    HC = V_C // HALVES
    assert all(tables[r].shape[0] == V for r in RESIDENT) and V_K * V_C == V and HC * HALVES == V_C
    assert V <= 2048

    A_UNITS = -(-(NF - 1) // TQ)
    UNITS = [("rows", i) for i in range(A_UNITS)] + [("pairs", i) for i in range(ZC)] \
        + [("layer1", i) for i in range(C1)] + [("layer2", i) for i in range(C2)] + [("layer3", 0)]
    NU = len(UNITS)
    ROWS_DONE, PAIRS_DONE, L1_DONE, L2_DONE = A_UNITS, A_UNITS + ZC, A_UNITS + ZC + C1, NU - 1
    W_BANKS = 3
    UNIT_ENGINE = ["VS"[i % 2] if k in ("rows", "pairs") else "S" for k, i in UNITS]

    def emptied_by(engine, n):
        return sum(e == engine for e in UNIT_ENGINE[:n])

    def lookup(o, count):
        plan = [("I", o + 2)] if o + 2 < count else []
        if count == NR:
            plan += [("M", o + 1, h) for h in range(HALVES) if o + 1 < NR]
            plan += [("R", o + 2, h) for h in range(HALVES) if o + 2 < NR]
        if o + 1 < count:
            plan += [("H", o + 1, h) for h in range(HALVES)]
        return plan + [("O", o)]

    def body_steps():
        plan = []
        for k in range(G_FILLS):
            plan.append(("G", -1, k))
            if k == 2:
                plan += [("I", 0), ("I", 1)] + [("H", 0, h) for h in range(HALVES)]
        units = [("W", n) for n in range(NU)]
        groups = [units[:3], units[3:PAIRS_DONE], units[PAIRS_DONE:L1_DONE], units[L1_DONE:]]
        for o in range(NK):
            plan += lookup(o, NK)
            todo = groups.pop(0) if groups else []
            fills = [("T", max(o - 2, 0), k) for k in range(T_FILLS)] if o >= 2 else []
            for i in range(max(len(todo), len(fills))):
                plan += fills[i:i + 1] + todo[i:i + 1]
        for t in range(TPB - 1):
            for k in range(G_FILLS):
                if t > 0 and k < T_FILLS:
                    plan.append(("T", t + 1, k))
                plan.append(("G", t, k))
        return plan + [("D",)]

    def first_steps():
        plan = [("R", 0, h) for h in range(HALVES)] + [("I", 0)] + [("M", 0, h) for h in range(HALVES)]
        plan += [("H", 0, h) for h in range(HALVES)] + [("I", 1)] + [("R", 1, h) for h in range(HALVES)]
        for k in range(NR):
            plan += lookup(k, NR)
            if k >= NR - T_FILLS:
                plan.append(("T", 0, k - (NR - T_FILLS)))
        for t in range(TPB - 1):
            for k in range(G_FILLS):
                if k < T_FILLS:
                    plan.append(("T", t + 1, k))
                plan.append(("G", t, k))
        return plan + [("D",)]

    FIRST, BODY = first_steps(), body_steps()
    LAST = [("G", -1, k) for k in range(G_FILLS)] + [("W", n) for n in range(NU)]

    with ExitStack() as ctx:
        def sb(name, shape, dt=F32):
            return ctx.enter_context(nc.sbuf_tensor(name, shape, dt))

        def bank(name):
            return ctx.enter_context(nc.psum_tensor(name, [P, 512], F32))

        def sem(name):
            return ctx.enter_context(nc.semaphore(name))

        idx = sb("idx", [P, TPB, n_tab], I32)
        rows = sb("rows", [P, TPB, len(turned), P])
        emb_t = sb("emb_t", [P, TPB, P, 32])
        dense_t = sb("dense_t", [P, COLS])
        gram = sb("gram", [P, TPB * U, NF])
        h1_pairs = sb("h1_pairs", [P, C1 * COLS])
        pair_rows = h1_pairs[:, 0:J * NP].rearrange("p (j z) -> p j z", j=J)
        h1 = h1_pairs[:].rearrange("p (c n) -> p c n", c=C1)
        h2_pairs = sb("h2_pairs", [P, ZC * COLS])
        pair_cols = h2_pairs[0:ZK, :].rearrange("p (c n) -> p c n", c=ZC)
        h2 = h2_pairs[:, 0:C2 * COLS].rearrange("p (c n) -> p c n", c=C2)
        w1z = sb("w1z", [ZK, ZC, H1])
        w1d = sb("w1d", [P, H1])
        w2s = sb("w2s", [P, C1, H2])
        w3s = sb("w3s", [P, C2])
        b1s = sb("b1s", [P, C1])
        b2s = sb("b2s", [P, C2])
        y = sb("y", [1, COLS])
        ident = sb("ident", [P, P])
        parts_sb = sb("parts", [V_K, NR - 2, 3 * V_C * P], BF16)
        parts = [parts_sb[:, r, :] for r in range(NR - 2)] \
            + [x[0:V_K, 0:3 * V_C * P // 2].bitcast(BF16) for x in (h1_pairs, h2_pairs)]
        parts = [x.rearrange("p (i c d) -> p i c d", i=3, c=V_C) for x in parts]
        onehot = sb("onehot", [V_K, HALVES, HC, COLS], BF16)
        ids_row = sb("ids_row", [P, 2, COLS], I32)
        ids_f16 = sb("ids_f16", [P, 2, COLS], F16)
        row_i32 = sb("row_i32", [V_K, V_C], I32)
        row_f32 = sb("row_f32", [V_K, V_C])

        scratch = gram[:].rearrange("p s b -> p (s b)")
        table_in = [scratch[0:V_K, i * V_C * P:(i + 1) * V_C * P] for i in range(2)]
        rest = scratch[0:V_K, 2 * V_C * P:3 * V_C * P]
        w1_second = h1_pairs[:, C1 * COLS - H1:]
        assert 3 * V_C * P // 2 <= min(ZC * COLS, C1 * COLS - H1)
        assert TPB * U * NF >= 3 * V_C * P

        t_bank = [bank(f"t_bank{i}") for i in range(2)]
        g_bank = [bank(f"g_bank{i}") for i in range(2)]
        w_bank = [bank(f"w_bank{i}") for i in range(W_BANKS)]
        o_bank = bank("o_bank")

        idx_loaded = [sem(f"idx_loaded{t}") for t in range(TPB)]
        dense_loaded = [sem(f"dense_loaded{t}") for t in range(TPB)]
        gathered = [[sem(f"gathered{t}_{k}") for k in range(T_FILLS)] for t in range(TPB)]
        rows_free = sem("rows_free")
        weights_loaded = sem("weights_loaded")
        table_loaded = [sem(f"table_loaded{i}") for i in range(2)]
        high_made = sem("high_made")
        rest_made = sem("rest_made")
        mid_made = sem("mid_made")
        low_made = sem("low_made")
        ids_loaded = [sem(f"ids_loaded{i}") for i in range(2)]
        ids_turned = sem("ids_turned")
        numbers_made = sem("numbers_made")
        row_ready = sem("row_ready")
        onehot_made = sem("onehot_made")
        onehot_used = sem("onehot_used")
        looked_up = sem("looked_up")
        lookup_by_s = sem("lookup_by_s")
        ident_zeroed = sem("ident_zeroed")
        ident_ready = sem("ident_ready")
        pad_zeroed = sem("pad_zeroed")
        w1d_ready = sem("w1d_ready")
        transposed = sem("transposed")
        emb_by_v = sem("emb_by_v")
        emb_by_s = sem("emb_by_s")
        dense_t_ready = sem("dense_t_ready")
        multiplied = sem("multiplied")
        gram_by_v = sem("gram_by_v")
        gram_by_s = sem("gram_by_s")
        unit_filled = sem("unit_filled")
        unit_by_v = sem("unit_by_v")
        unit_by_s = sem("unit_by_s")
        stored = sem("stored")

        NT = TPB * T_FILLS
        NG = TPB * G_FILLS
        assert T_FILLS % 2 == 0 and NG % 2 == 0
        N_WEIGHTS = 7

        dense_tiles = dense.rearrange("(p n) d -> p n d", n=TILES)
        ids_tiles = ids.rearrange("(p n) f -> p n f", n=TILES)
        out_tiles = out.rearrange("(p n) one -> p (n one)", n=TILES)

        def gathers(b, k):
            return (len([f for f in FIRST_FILLS[k] if f > 0])) + len([f for f in FILLS[k] if f > 0]) * b

        def lookups(b, o, first):
            return o if first else NR - NK + NK * b + o

        def slot_loads(b, o, first):
            if first:
                return o // 2 + 1
            per_block = len(range(o % 2, NK, 2))
            return len(range(o % 2, NR, 2)) - per_block + per_block * b + o // 2 + 1

        def blocks(eng, body):
            body(0, FIRST)
            with eng.Fori(1, BLOCKS) as b:
                body(b, BODY)
            body(BLOCKS, LAST)

        def load_table(eng, r):
            eng.dma_start(table_in[r % 2], tables[RESIDENT[r]].rearrange("(q c) d -> q (c d)", c=V_C)
                          ).then_inc(table_loaded[r % 2], 16)

        def half(x, h):
            return x[:, h * HC * P:(h + 1) * HC * P]

        def part(r, i, h):
            return half(parts[r][:, i].rearrange("p c d -> p (c d)"), h)

        block = ctx.enter_context(nc.Block())

        @block.sync
        def _(sp):
            def load_idx(b, t):
                sp.dma_start(idx[:, t, :], ids_tiles[:, bass.ds(b * TPB + t, 1), :].rearrange("p n f -> p (n f)")
                             ).then_inc(idx_loaded[t], 16)

            def load_dense(b, t):
                sp.dma_start(rows[:, t, 0, :], dense_tiles[:, bass.ds(b * TPB + t, 1), :].rearrange("p n d -> p (n d)")
                             ).then_inc(dense_loaded[t], 16)

            def load_tile(b, t):
                sp.wait_ge(transposed, NT * (b - 1) + T_FILLS * (t + 1))
                load_idx(b, t)
                load_dense(b, t)

            def load_ids(b, o, first=False):
                if not first or o >= 2:
                    sp.wait_ge(ids_turned, lookups(b, max(o - 1, 0), first))
                row = ids_t[RESIDENT[o]:RESIDENT[o] + 1, bass.ds(COLS * b, COLS)]
                sp.dma_start(ids_row[:, o % 2, :], row.partition_broadcast(P).rearrange("p o n -> p (o n)")
                             ).then_inc(ids_loaded[o % 2], 16)

            load_idx(0, 0)
            for r in range(2):
                load_ids(0, r, True)
            for t in range(1, TPB):
                load_idx(0, t)
            for r in range(2, NR):
                sp.wait_ge(low_made, HALVES * (r - 1))
                load_table(sp, r)
                load_ids(0, r, True)
                if r - 2 < TPB:
                    load_dense(0, r - 2)
            for dst, src in (
                (w1z[:], w1[P:P + NP, :].rearrange("(c p) n -> p c n", p=ZK)),
                (w1d[:], w1[0:P, :]), (w1_second, w1[P + NP:, :]),
                (w2s[:], w2.rearrange("(p c) n -> p c n", c=C1)),
                (w3s[:], w3.rearrange("(p c) one -> p (c one)", c=C2)),
                (b1s[:], b1.rearrange("(p c) -> p c", c=C1)),
                (b2s[:], b2.rearrange("(p c) -> p c", c=C2)),
            ):
                sp.dma_start(dst, src).then_inc(weights_loaded, 16)
            with sp.Fori(1, BLOCKS) as b:
                load_tile(b, 0)
                load_ids(b, 0)
                load_ids(b, 1)
                for t in range(1, TPB):
                    load_tile(b, t)
                for o in range(2, NK):
                    load_ids(b, o)
            sp.wait_ge(stored, 16 * BLOCKS)

        @block.gpsimd
        def _(pool):
            def gather_block(b, again, ts=range(TPB)):
                for t in ts:
                    pool.wait_ge(idx_loaded[t], 16 * (b + 1))
                    for k in range(T_FILLS):
                        if again:
                            pool.wait_ge(transposed, NT * (b - 1) + T_FILLS * t + k + 1)
                            pool.sem_inc(rows_free, 1)
                        for f in FILLS[k] if again else FIRST_FILLS[k]:
                            if f > 0:
                                nc.gpsimd.indirect_dma_start(
                                    rows[:, t, SLOT[f], :], None, tables[f - 1],
                                    bass.IndirectOffsetOnAxis(ap=idx[:, t, f - 1:f], axis=0),
                                ).then_inc(gathered[t][k], 16)

            nc.gpsimd.iota(row_i32[:], pattern=[[1, V_C]], base=0, channel_multiplier=V_C).then_inc(numbers_made, 1)
            nc.gpsimd.memset(ident[:], 0.0).then_inc(ident_zeroed, 1)
            pool.wait_ge(ident_zeroed, 1)
            nc.gpsimd.affine_select(out=ident[:], in_=ident[:], compare_op=ALU.not_equal, fill=1.0,
                                    base=0, pattern=[[-1, P]], channel_multiplier=1).then_inc(ident_ready, 1)
            gather_block(0, False)
            with pool.Fori(1, BLOCKS) as b:
                gather_block(b, True)

        @block.tensor
        def _(pe):
            def transposes(b, t, k, first):
                n = T_FILLS * t + k
                if k == 0:
                    pe.wait_ge(dense_loaded[t], 16 * (b + 1))
                pe.wait_ge(gathered[t][k], 16 * gathers(b, k))
                if n >= 2 or not first:
                    pe.wait_ge(emb_by_s if n % 2 else emb_by_v, NT // 2 * b + n // 2)
                for i, f in enumerate(FIRST_FILLS[k] if first else FILLS[k]):
                    last = nc.tensor.transpose(t_bank[n % 2][:, i * P:(i + 1) * P], rows[:, t, SLOT[f], :], ident[:])
                last.then_inc(transposed, 1)

            def products(b, t, k, first):
                m = G_FILLS * t + k
                if k == 0:
                    n = T_FILLS * (t + 1)
                    pe.wait_ge(emb_by_v, NT // 2 * b + n // 2)
                    pe.wait_ge(emb_by_s, NT // 2 * b + n // 2)
                    if t == 0:
                        pe.wait_ge(lookup_by_s, lookups(b, NR if first else NK, first))
                if not (first and m < 2):
                    pe.wait_ge(gram_by_v, NG * b + m - 1)
                    pe.wait_ge(gram_by_s, NG * b + m - 1)
                for i in range(GQ):
                    group = emb_t[:, t % TPB, J * (GQ * k + i):J * (GQ * k + i + 1), :]
                    last = nc.tensor.matmul(g_bank[m % 2][0:GP, i * J * NF:(i + 1) * J * NF],
                                            group.rearrange("p j f -> p (j f)")[:, 0:GP], group[:, :, 0:NF],
                                            start=True, stop=True)
                last.then_inc(multiplied, 1)

            def select(b, o, first):
                if not first or o > 0:
                    pe.wait_ge(lookup_by_s, lookups(b, o, first))
                for h in range(HALVES):
                    if first:
                        pe.wait_ge(low_made, HALVES * o + h + 1)
                    pe.wait_ge(onehot_made, HALVES * lookups(b, o, first) + h + 1)
                    for c in range(HC):
                        for part in range(3):
                            last = nc.tensor.matmul(o_bank[:], parts[o][:, part, HC * h + c, :], onehot[:, h, c, :],
                                                    start=(h == c == part == 0),
                                                    stop=(h == HALVES - 1 and c == HC - 1 and part == 2))
                    if h < HALVES - 1:
                        last.then_inc(onehot_used, 1)
                last.then_inc(looked_up, 1)

            def unit(b, n):
                kind, i = UNITS[n]
                to = w_bank[n % W_BANKS]
                done = b - 1
                if n == 0:
                    pe.wait_ge(unit_by_s, emptied_by("S", NU) * done + 1)
                if n >= W_BANKS:
                    last_fill = n - W_BANKS
                    if UNIT_ENGINE[last_fill] == "V":
                        pe.wait_ge(unit_by_v, emptied_by("V", NU) * done + emptied_by("V", last_fill + 1))
                    else:
                        pe.wait_ge(unit_by_s, emptied_by("S", NU) * done + emptied_by("S", last_fill + 1) + 1)
                if kind == "rows":
                    if i == 0:
                        pe.wait_ge(gram_by_v, NG * b)
                        pe.wait_ge(gram_by_s, NG * b)
                    for q, a in enumerate(range(TQ * i, min(TQ * i + TQ, NF - 1))):
                        last = nc.tensor.transpose(to[:, q * P:q * P + GP], gram[0:GP, :, a], ident[0:GP, 0:GP])
                elif kind == "pairs":
                    if i == 0:
                        pe.wait_ge(unit_by_v, emptied_by("V", NU) * done + emptied_by("V", ROWS_DONE))
                        pe.wait_ge(unit_by_s, emptied_by("S", NU) * done + emptied_by("S", ROWS_DONE) + 1)
                    for j in range(J):
                        last = nc.tensor.transpose(to[0:ZK, j * P:(j + 1) * P],
                                                   pair_rows[:, j, i * ZK:(i + 1) * ZK], ident[:])
                elif kind == "layer1":
                    if i == 0:
                        pe.wait_ge(dense_t_ready, b)
                    cols = slice(i, H1, C1)
                    nc.tensor.matmul(to[:], w1d[:, cols], dense_t[:], start=True, stop=False)
                    if i == 0:
                        pe.wait_ge(unit_by_v, emptied_by("V", NU) * done + emptied_by("V", PAIRS_DONE))
                        pe.wait_ge(unit_by_s, emptied_by("S", NU) * done + emptied_by("S", PAIRS_DONE) + 1)
                    for c in range(ZC):
                        last = nc.tensor.matmul(to[:], w1z[:, c, cols], pair_cols[:, c, :],
                                                start=False, stop=(c == ZC - 1))
                elif kind == "layer2":
                    for c in range(C1):
                        if i == 0 and c in (0, C1 - 1):
                            pe.wait_ge(unit_by_s, emptied_by("S", NU) * done + emptied_by("S", L1_DONE) + (c > 0))
                        last = nc.tensor.matmul(to[:], w2s[:, c, i:H2:C2], h1[:, c, :],
                                                start=(c == 0), stop=(c == C1 - 1))
                else:
                    for c in range(C2):
                        pe.wait_ge(unit_by_s, emptied_by("S", NU) * done + emptied_by("S", L2_DONE) - C2 + c + 2)
                        last = nc.tensor.matmul(to[0:1, :], w3s[:, c:c + 1], h2[:, c, :],
                                                start=(c == 0), stop=(c == C2 - 1))
                last.then_inc(unit_filled, 1)

            def body(b, plan):
                first = plan is FIRST
                for kind, *at in plan:
                    if kind == "T":
                        transposes(b, *at, first)
                    elif kind == "G":
                        if first and at == [0, 0]:
                            pe.wait_ge(pad_zeroed, 1)
                        products(b, *at, first)
                    elif kind == "O":
                        select(b, *at, first)
                    elif kind == "W":
                        unit(b, *at)
                if first:
                    pe.wait_ge(weights_loaded, 16 * N_WEIGHTS)
                    pe.wait_ge(w1d_ready, 1)

            pe.wait_ge(ident_ready, 1)
            blocks(pe, body)

        def empty_tile_bank(eng, b, t, k, first):
            n = T_FILLS * t + k
            fs = FIRST_FILLS[k] if first else FILLS[k]
            eng.wait_ge(transposed, NT * b + n + 1)
            src = t_bank[n % 2][:, 0:len(fs) * P].rearrange("p (f s) -> p s f", f=len(fs))
            return emb_t[:, t, :, fs[0]:fs[-1] + 1], src

        def gram_part(m, t, k, j):
            q = slice(32 * j, min(32 * j + 32, GP))
            src = g_bank[m % 2][:, 0:GQ * J * NF].rearrange("p (g j b) -> p g j b", g=GQ, j=J)
            s = U * (t % TPB) + GQ * k
            return gram[q, s:s + GQ, :], src[q, :, j, :]

        def unit_bank(eng, b, n):
            eng.wait_ge(unit_filled, NU * (b - 1) + n + 1)
            return w_bank[n % W_BANKS]

        def empty_unit(copy, n, src):
            work, i = UNITS[n]
            if work == "pairs":
                return copy(pair_cols[:, i, :], src[0:ZK, :])
            for q, a in enumerate(range(TQ * i, min(TQ * i + TQ, NF - 1))):
                first_pair = a * NF - a * (a + 1) // 2
                block_a = src[:, q * P:(q + 1) * P].rearrange("p (j b) -> p j b", j=J)
                last = copy(pair_rows[:, :, first_pair:first_pair + NF - 1 - a], block_a[:, :, a + 1:NF])
            return last

        @block.vector
        def _(dve):
            def cut_rest(r, h):
                dve.wait_ge(high_made, HALVES * r + h + 1)
                if r > 0:
                    dve.wait_ge(low_made, HALVES * (r - 1) + h + 1)
                nc.vector.tensor_tensor(half(rest, h), half(table_in[r % 2], h), part(r, 0, h), ALU.subtract
                                        ).then_inc(rest_made, 1)

            def cut_low(r, h):
                dve.wait_ge(mid_made, HALVES * r + h + 1)
                nc.vector.tensor_tensor(part(r, 2, h), half(rest, h), part(r, 1, h), ALU.subtract
                                        ).then_inc(low_made, 1)

            def one_hot(b, o, h, first):
                if h == 0:
                    dve.wait_ge(ids_turned, lookups(b, o, first) + 1)
                if not first or o > 0:
                    if h < HALVES - 1:
                        dve.wait_ge(onehot_used, lookups(b, o, first))
                    else:
                        dve.wait_ge(looked_up, lookups(b, o, first))
                for c in range(HC):
                    at = HC * h + c
                    last = nc.vector.tensor_scalar(onehot[:, h, c, :], ids_f16[0:V_K, o % 2, :],
                                                   row_f32[:, at:at + 1], None, ALU.is_equal)
                last.then_inc(onehot_made, 1)

            dve.wait_ge(numbers_made, 1)
            nc.vector.tensor_copy(row_f32[:], row_i32[:]).then_inc(row_ready, 1)
            nc.vector.memset(emb_t[:, :, :, NF:], 0.0).then_inc(pad_zeroed, 1)
            dve.wait_ge(row_ready, 1)

            def body(b, plan):
                first = plan is FIRST
                for kind, *at in plan:
                    if kind == "T":
                        t, k = at
                        if (T_FILLS * t + k) % 2 == 0:
                            if not first and t == k == 0:
                                dve.wait_ge(dense_t_ready, b)
                            dst, src = empty_tile_bank(dve, b, t, k, first)
                            nc.vector.tensor_copy(dst, src).then_inc(emb_by_v, 1)
                    elif kind == "G":
                        t, k = at
                        m = G_FILLS * t + k
                        dve.wait_ge(multiplied, NG * b + m + 1)
                        for j in (0, 1):
                            last = nc.vector.tensor_copy(*gram_part(m, t, k, j))
                        last.then_inc(gram_by_v, 1)
                    elif kind == "R":
                        cut_rest(*at)
                    elif kind == "M":
                        cut_low(*at)
                    elif kind == "H":
                        one_hot(b, *at, first)
                    elif kind == "W" and UNIT_ENGINE[at[0]] == "V":
                        empty_unit(nc.vector.tensor_copy, at[0], unit_bank(dve, b, at[0])).then_inc(unit_by_v, 1)
                if first:
                    dve.wait_ge(weights_loaded, 16 * N_WEIGHTS)
                    nc.vector.tensor_tensor(w1d[:], w1d[:], w1_second, ALU.add).then_inc(w1d_ready, 1)
                    dve.wait_ge(w1d_ready, 1)

            blocks(dve, body)

        @block.scalar
        def _(act):
            def cut_high(r, h):
                if h == 0:
                    act.wait_ge(table_loaded[r % 2], 16 * (r // 2 + 1))
                nc.scalar.copy(part(r, 0, h), half(table_in[r % 2], h)).then_inc(high_made, 1)

            def cut_middle(r, h):
                act.wait_ge(rest_made, HALVES * r + h + 1)
                nc.scalar.copy(part(r, 1, h), half(rest, h)).then_inc(mid_made, 1)

            for r in range(2):
                load_table(act, r)

            def body(b, plan):
                first = plan is FIRST
                for kind, *at in plan:
                    if kind == "T":
                        t, k = at
                        if (T_FILLS * t + k) % 2 == 1:
                            dst, src = empty_tile_bank(act, b, t, k, first)
                            nc.scalar.copy(dst, src).then_inc(emb_by_s, 1)
                    elif kind == "G":
                        t, k = at
                        m = G_FILLS * t + k
                        act.wait_ge(multiplied, NG * b + m + 1)
                        for j in (2, 3):
                            last = nc.scalar.copy(*gram_part(m, t, k, j))
                        last.then_inc(gram_by_s, 1)
                    elif kind == "I":
                        o, = at
                        act.wait_ge(ids_loaded[o % 2], 16 * slot_loads(b, o, first))
                        if not first or o >= 2:
                            act.wait_ge(onehot_made, HALVES * lookups(b, max(o - 1, 0), first))
                        nc.scalar.copy(ids_f16[:, o % 2, :], ids_row[:, o % 2, :]).then_inc(ids_turned, 1)
                    elif kind == "R":
                        cut_high(*at)
                    elif kind == "M":
                        cut_middle(*at)
                    elif kind == "O":
                        o, = at
                        act.wait_ge(looked_up, lookups(b, o, first) + 1)
                        nc.scalar.copy(emb_t[:, :, :, RESIDENT[o] + 1],
                                       o_bank[:].rearrange("p (t s) -> p t s", t=TPB)).then_inc(lookup_by_s, 1)
                    elif kind == "D":
                        if not first:
                            act.wait_ge(stored, 16 * b)
                            act.wait_ge(unit_filled, NU * (b - 1) + L1_DONE)
                        act.wait_ge(emb_by_v, NT // 2 * b + T_FILLS // 2 * (TPB - 1) + 1)
                        for t in range(TPB):
                            last = nc.scalar.copy(
                                dense_t[:].rearrange("p (j t u) -> p t j u", j=J, t=TPB)[:, t],
                                emb_t[:, t, :, 0].rearrange("p (u j) -> p j u", j=J))
                        last.then_inc(dense_t_ready, 1)
                    elif kind == "W" and UNIT_ENGINE[at[0]] == "S":
                        work, i = UNITS[at[0]]
                        src = unit_bank(act, b, at[0])
                        if work == "layer1":
                            last = nc.scalar.activation(h1[:, i, :], src[:], ACT.Relu, bias=b1s[:, i:i + 1])
                        elif work == "layer2":
                            last = nc.scalar.activation(h2[:, i, :], src[:], ACT.Relu, bias=b2s[:, i:i + 1])
                        elif work != "layer3":
                            last = empty_unit(nc.scalar.copy, at[0], src)
                        else:
                            last = nc.scalar.copy(y[:].rearrange("o (u j t) -> o j t u", j=J, t=TPB),
                                                  src[0:1, :].rearrange("o (j t u) -> o j t u", j=J, t=TPB))
                        last.then_inc(unit_by_s, 1)
                        if work == "layer3":
                            act.wait_ge(unit_by_s, emptied_by("S", NU) * b + 1)
                            act.dma_start(out_tiles[:, bass.ds(TPB * (b - 1), TPB)],
                                          y[:].rearrange("o (q t) -> o q t", t=TPB)).then_inc(stored, 16)
                if first:
                    act.wait_ge(weights_loaded, 16 * N_WEIGHTS)
                    nc.scalar.copy(y[:, 0:1], b1s[0:1, 0:1]).then_inc(unit_by_s, 1)

            blocks(act, body)


N_TABLES = 26
_INS = ["r_dense_features", "ids"] + [f"tbl_{i}" for i in range(N_TABLES)] + ["W_top1", "b_top1", "W_top2", "b_top2", "W_top3"]


def kernel(**inputs):
    import numpy as _np
    import concourse.bacc as _bacc
    from concourse import mybir as _mybir
    from concourse.bass_utils import run_bass_kernel_spmd as _run

    nc = _bacc.Bacc("TRN2", target_bir_lowering=False, num_devices=1)
    arrays, aps = {}, {}
    for name in _INS:
        a = _np.ascontiguousarray(inputs[name])
        arrays[f"in_{name}"] = a
        aps[name] = nc.dram_tensor(f"in_{name}", a.shape, _mybir.dt.from_np(a.dtype), kind="ExternalInput").ap()
    batch, n_tab = arrays["in_ids"].shape
    a = _np.ascontiguousarray(arrays["in_ids"].reshape(P, batch // P, n_tab).transpose(2, 1, 0).reshape(n_tab, batch))
    arrays["in_ids_t"] = a
    ids_t = nc.dram_tensor("in_ids_t", a.shape, _mybir.dt.from_np(a.dtype), kind="ExternalInput").ap()
    out = nc.dram_tensor("out_y", (batch, 1), F32, kind="ExternalOutput").ap()
    dlrm_tower(nc, aps["r_dense_features"], aps["ids"], ids_t, [aps[f"tbl_{i}"] for i in range(N_TABLES)],
               aps["W_top1"], aps["b_top1"], aps["W_top2"], aps["b_top2"], aps["W_top3"], out)
    r = _run(nc, [arrays], core_ids=[0])
    return r.results[0]["out_y"]
```

```python
from contextlib import ExitStack

import concourse.bass as bass
from concourse import mybir

F32 = mybir.dt.float32
F16 = mybir.dt.float16
BF16 = mybir.dt.bfloat16
I32 = mybir.dt.int32
ACT = mybir.ActivationFunctionType
ALU = mybir.AluOpType

P = 128
RESIDENT = (3, 8, 9, 2, 25, 10, 14, 24)
FROM_TILE = {"first": (0, 0, 0, 0, 0, 0, 0, 0), "middle": (0, 0, 0, 0, 0, 4, 4, 4), "last": (0, 0, 0, 4, 4, 4, 4, 4)}


def dlrm_tower(nc, dense, ids, ids_t, tables, w1, b1, w2, b2, w3, out):
    batch, d_emb = dense.shape
    n_tab = len(tables)
    NF = n_tab + 1
    NP = NF * (NF - 1) // 2
    TILES = batch // P
    TPB = 4
    BLOCKS = TILES // TPB
    COLS = TPB * P
    J = 4
    U = P // J
    GP = 32 * (J - 1) + NF
    H1, H2 = w2.shape
    C1, C2 = H1 // P, H2 // P
    ZC = 3
    ZK = NP // ZC
    assert d_emb == P and ZK * ZC == NP and w1.shape[0] == 2 * P + NP

    TQ = 4
    ALWAYS = [r for i, r in enumerate(RESIDENT) if not any(FROM_TILE[share][i] for share in FROM_TILE)]
    N_LOOKUPS = {share: sum(t < TPB for t in FROM_TILE[share]) for share in FROM_TILE}
    NR, NK = len(RESIDENT), N_LOOKUPS["middle"]
    turned = [f for f in range(NF) if f - 1 not in ALWAYS]
    FILLS = []
    for f in turned:
        if FILLS and len(FILLS[-1]) < TQ and FILLS[-1][-1] == f - 1:
            FILLS[-1].append(f)
        else:
            FILLS.append([f])
    T_FILLS = len(FILLS)

    def in_fill(t, k, share):
        return [f for f in FILLS[k] if f - 1 not in RESIDENT or t < FROM_TILE[share][RESIDENT.index(f - 1)]]

    for share in FROM_TILE:
        for fs in [in_fill(t, k, share) for t in range(TPB) for k in range(T_FILLS)]:
            assert fs and fs[-1] - fs[0] == len(fs) - 1

    SLOT = {f: i for i, f in enumerate(turned)}
    GQ = 4
    G_FILLS = U // GQ

    V = tables[RESIDENT[0]].shape[0]
    V_C = -(-V // P)
    V_K = V // V_C
    HALVES = 2
    HC = V_C // HALVES
    assert all(tables[r].shape[0] == V for r in RESIDENT) and V_K * V_C == V and HC * HALVES == V_C
    assert V <= 2048

    A_UNITS = -(-(NF - 1) // TQ)
    UNITS = [("rows", i) for i in range(A_UNITS)] + [("pairs", i) for i in range(ZC)] \
        + [("layer1", i) for i in range(C1)] + [("layer2", i) for i in range(C2)] + [("layer3", 0)]
    NU = len(UNITS)
    ROWS_DONE, PAIRS_DONE, L1_DONE, L2_DONE = A_UNITS, A_UNITS + ZC, A_UNITS + ZC + C1, NU - 1
    W_BANKS = 2
    G_BANKS = 3
    UNIT_ENGINE = ["VS"[i % 2] if k in ("rows", "pairs") else "S" for k, i in UNITS]

    def emptied_by(engine, n):
        return sum(e == engine for e in UNIT_ENGINE[:n])

    def row_numbers(o, count):
        return [("I", o)] if o < count else []

    def units_of(part):
        return [("W", n, part) for n in range(NU)]

    def body_steps(last=False):
        plan = []
        NK = N_LOOKUPS["last" if last else "middle"]
        for k in range(G_FILLS):
            plan.append(("G", -1, k))
            plan += {1: [("I", 0)], 3: [("H", 0, 0)], 5: [("I", 1)], 7: [("H", 0, 1)]}.get(k, [])
        units = units_of(None)
        per_slot = [2, 2, 1, 2, 2, 1] if last else [2, 2, 1, 2, 0, 2, 1, 1, 0, 1]
        for x in range(HALVES * NK):
            o, h = divmod(x, HALVES)
            if h == 0:
                plan += row_numbers(o + 2, NK)
            plan.append(("O", o, h))
            if o + 1 < NK:
                plan.append(("H", o + 1, h))
            plan += units[:per_slot[x]]
            del units[:per_slot[x]]
        fills = [("T", 0, k) for k in range(T_FILLS)]
        for n in (1, 1, 1, 1, 1, 1) if last else (1, 2, 2, 1):
            plan += fills[:n] + units[:1]
            del fills[:n], units[:1]
        tiles = tile_steps()
        plan += tiles[:1] + [("V", None)] + tiles[1:6] + units
        if not last:
            return plan + tiles[6:]
        units = units_of(0)
        t2, t3 = [[("T", t, k) for k in range(T_FILLS)] for t in (TPB - 2, TPB - 1)]
        g2 = [("G", TPB - 2, k) for k in range(G_FILLS)]
        half_done = tiles.index(g2[0])
        late = t2[3:]
        plan += [step for step in tiles[6:half_done] if step not in late] + [("D", 0)]
        for pattern in "tWWtWtWWWW", "gWgWgWg", "WgWTWgTWTWTgWTvgT", "W":
            for step in pattern:
                plan.append(("V", 0) if step == "v" else {"W": units, "t": late, "T": t3, "g": g2}[step].pop(0))
        return plan + [("D", 1)]

    def tile_steps():
        plan = []
        for t in range(TPB - 1):
            late = {0: -1, TPB - 2: G_FILLS - T_FILLS}.get(t, 0)
            plan += [("T", t + 1, k) for k in range(-late)]
            for k in range(G_FILLS):
                if late <= k < T_FILLS + late:
                    plan.append(("T", t + 1, k - late))
                plan.append(("G", t, k))
        return plan + [("D", None)]

    def first_steps():
        plan = [("R", 0, 0), ("I", 0), ("H", 0, 0), ("M", 0, 0), ("R", 0, 1), ("M", 0, 1), ("H", 0, 1)]
        plan += [("I", 1), ("R", 1, 0)]

        def ahead(kind, o, h, n):
            q = HALVES * o + h + n
            return [(kind, *divmod(q, HALVES))] if q < HALVES * NR else []

        for o in range(NR):
            for h in range(HALVES):
                plan += ahead("R", o, h, 3) * (o > 0 or h > 0) + ahead("M", o, h, 2)
                plan += [("O", o, h)] + ahead("H", o, h, 2) + ahead("R", o, h, 3) * (o == h == 0)
            plan += row_numbers(o + 2, NR)
            if o >= NR - T_FILLS:
                plan.append(("T", 0, o - (NR - T_FILLS)))
        tiles = tile_steps()
        return plan + tiles[:-8] + [("A",)] + tiles[-8:]

    FIRST, BODY, SPLIT = first_steps(), body_steps(), body_steps(last=True)
    LAST = [("G", -1, k) for k in range(G_FILLS)] + [("P", 0), ("P", 1)] + units_of(1)[:ROWS_DONE] + [("P", 2)] \
        + units_of(1)[ROWS_DONE:PAIRS_DONE] + [("P", 3)] + units_of(1)[PAIRS_DONE:]

    with ExitStack() as ctx:
        def sb(name, shape, dt=F32):
            return ctx.enter_context(nc.sbuf_tensor(name, shape, dt))

        def bank(name):
            return ctx.enter_context(nc.psum_tensor(name, [P, 512], F32))

        def sem(name):
            return ctx.enter_context(nc.semaphore(name))

        idx = sb("idx", [P, TPB, n_tab], I32)
        rows = sb("rows", [P, TPB, len(turned), P])
        emb_t = sb("emb_t", [P, TPB, P, 32])
        dense_t = sb("dense_t", [P, COLS])
        gram = sb("gram", [P, TPB * U, NF])
        h1_pairs = sb("h1_pairs", [P, C1 * COLS])
        pair_rows = h1_pairs[:, 0:J * NP].rearrange("p (j z) -> p j z", j=J)
        h1 = h1_pairs[:].rearrange("p (c n) -> p c n", c=C1)
        h2_pairs = sb("h2_pairs", [P, ZC * COLS])
        pair_cols = h2_pairs[0:ZK, :].rearrange("p (c n) -> p c n", c=ZC)
        h2 = h2_pairs[:, 0:C2 * COLS].rearrange("p (c n) -> p c n", c=C2)
        w1z = sb("w1z", [ZK, ZC, H1])
        w1d = sb("w1d", [P, H1])
        w2s = sb("w2s", [P, C1, H2])
        w3s = sb("w3s", [P, C2])
        b1s = sb("b1s", [P, C1])
        b2s = sb("b2s", [P, C2])
        ones = sb("ones", [P, 1])
        y = sb("y", [1, COLS])
        ident = sb("ident", [P, P])
        parts_sb = sb("parts", [V_K, NR - 2, 3 * V_C * P], BF16)
        parts = [parts_sb[:, r, :] for r in range(NR - 2)] \
            + [x[0:V_K, 0:3 * V_C * P // 2].bitcast(BF16) for x in (h1_pairs, h2_pairs)]
        parts = [x.rearrange("p (i c d) -> p i c d", i=3, c=V_C) for x in parts]
        onehot = sb("onehot", [V_K, HALVES, HC, COLS], BF16)
        ids_row = sb("ids_row", [P, 2, COLS], I32)
        ids_f16 = sb("ids_f16", [P, 2, COLS], F16)
        row_i32 = sb("row_i32", [V_K, V_C], I32)
        row_f32 = sb("row_f32", [V_K, V_C])

        scratch = gram[:].rearrange("p s b -> p (s b)")
        table_in = [scratch[0:V_K, i * V_C * P:(i + 1) * V_C * P] for i in range(2)]
        rest = scratch[0:V_K, 2 * V_C * P:3 * V_C * P]
        w1_second = h1_pairs[:, C1 * COLS - H1:]
        assert 3 * V_C * P // 2 <= min(ZC * COLS, C1 * COLS - H1)
        assert TPB * U * NF >= 3 * V_C * P

        t_bank = [bank(f"t_bank{i}") for i in range(2)]
        g_bank = [bank(f"g_bank{i}") for i in range(G_BANKS)]
        w_bank = [bank(f"w_bank{i}") for i in range(W_BANKS)]
        o_bank = bank("o_bank")
        EARLY_BANKS = t_bank + g_bank[:2]
        FIRST_BANKS = [o_bank, w_bank[0]]
        LAST_BANKS = w_bank + [o_bank]

        idx_loaded = [sem(f"idx_loaded{t}") for t in range(TPB)]
        dense_loaded = [sem(f"dense_loaded{t}") for t in range(TPB)]
        gathered = [[sem(f"gathered{t}_{k}") for k in range(T_FILLS)] for t in range(TPB)]
        rows_free = sem("rows_free")
        weights_loaded = sem("weights_loaded")
        table_loaded = [[sem(f"table_loaded{i}_{h}") for h in range(HALVES)] for i in range(2)]
        high_made = sem("high_made")
        rest_made = sem("rest_made")
        mid_made = sem("mid_made")
        low_made = sem("low_made")
        ids_loaded = [sem(f"ids_loaded{i}") for i in range(2)]
        ids_turned = sem("ids_turned")
        numbers_made = sem("numbers_made")
        row_ready = sem("row_ready")
        onehot_made = sem("onehot_made")
        onehot_used = sem("onehot_used")
        looked_up = sem("looked_up")
        lookup_by_s = sem("lookup_by_s")
        ident_zeroed = sem("ident_zeroed")
        ident_ready = sem("ident_ready")
        pad_zeroed = sem("pad_zeroed")
        w1d_ready = sem("w1d_ready")
        transposed = sem("transposed")
        emb_by_v = sem("emb_by_v")
        emb_by_s = sem("emb_by_s")
        dense_t_ready = sem("dense_t_ready")
        multiplied = sem("multiplied")
        gram_by_v = sem("gram_by_v")
        gram_by_s = sem("gram_by_s")
        unit_filled = sem("unit_filled")
        unit_by_v = sem("unit_by_v")
        unit_by_s = sem("unit_by_s")
        h2_scaled = [sem(f"h2_scaled{c}") for c in range(C2 - 1)]
        h2_weighted = sem("h2_weighted")
        stored = sem("stored")

        NT = TPB * T_FILLS
        NG = TPB * G_FILLS
        assert T_FILLS % 2 == 0 and NG % 2 == 0
        N_WEIGHTS = 7
        CLOCK_STARTERS = 26

        dense_tiles = dense.rearrange("(p n) d -> p n d", n=TILES)
        ids_tiles = ids.rearrange("(p n) f -> p n f", n=TILES)
        out_tiles = out.rearrange("(p n) one -> p (n one)", n=TILES)

        def gathers(b, t, k, share):
            first, middle, last = [len([f for f in in_fill(t, k, x) if f > 0]) for x in ("first", "middle", "last")]
            return first + (middle * b if share != "last" else middle * (b - 1) + last)

        def share_of(plan):
            return "first" if plan is FIRST else "last" if plan is SPLIT else "middle"

        def lookups(b, o, first):
            return o if first else NR - NK + NK * b + o

        def rounds_done(b, part):
            return b - 1 if part is None else b

        def groups(part):
            return (0, TPB * U) if part is None else (part * TPB * U // 2, TPB * U // 2)

        def slot_loads(b, o, first):
            if first:
                return o // 2 + 1
            per_block = len(range(o % 2, NK, 2))
            return len(range(o % 2, NR, 2)) - per_block + per_block * b + o // 2 + 1

        def blocks(eng, body):
            body(0, FIRST)
            with eng.Fori(1, BLOCKS - 1) as b:
                body(b, BODY)
            body(BLOCKS - 1, SPLIT)
            body(BLOCKS, LAST)

        def half(x, h):
            return x[:, h * HC * P:(h + 1) * HC * P]

        def load_table(eng, r):
            for h in range(HALVES):
                eng.dma_start(half(table_in[r % 2], h), half(tables[RESIDENT[r]].rearrange("(q c) d -> q (c d)", c=V_C), h)
                              ).then_inc(table_loaded[r % 2][h], 16)

        def part(r, i, h):
            return half(parts[r][:, i].rearrange("p c d -> p (c d)"), h)

        def unit_banks(part):
            return w_bank if part is None else LAST_BANKS

        def unit_bank(n, part):
            kind, i = UNITS[n]
            return EARLY_BANKS[i] if part == 1 and kind == "layer1" else unit_banks(part)[n % len(unit_banks(part))]

        def lookup_bank(o, first):
            return FIRST_BANKS[o % 2] if first else o_bank

        block = ctx.enter_context(nc.Block())

        @block.sync
        def _(sp):
            def load_idx(b, t):
                sp.dma_start(idx[:, t, :], ids_tiles[:, bass.ds(b * TPB + t, 1), :].rearrange("p n f -> p (n f)")
                             ).then_inc(idx_loaded[t], 16)

            def load_dense(b, t):
                sp.dma_start(rows[:, t, 0, :], dense_tiles[:, bass.ds(b * TPB + t, 1), :].rearrange("p n d -> p (n d)")
                             ).then_inc(dense_loaded[t], 16)

            def load_tile(b, t):
                sp.wait_ge(transposed, NT * (b - 1) + T_FILLS * (t + 1))
                load_idx(b, t)
                load_dense(b, t)

            def load_block(b, share):
                load_tile(b, 0)
                load_ids(b, 0)
                load_ids(b, 1)
                for t in range(1, TPB):
                    load_tile(b, t)
                for o in range(2, N_LOOKUPS[share]):
                    load_ids(b, o)

            def load_ids(b, o, first=False):
                if not first or o >= 2:
                    sp.wait_ge(ids_turned, lookups(b, max(o - 1, 0), first))
                row = ids_t[RESIDENT[o]:RESIDENT[o] + 1, bass.ds(COLS * b, COLS)]
                sp.dma_start(ids_row[:, o % 2, :], row.partition_broadcast(P).rearrange("p o n -> p (o n)")
                             ).then_inc(ids_loaded[o % 2], 16)

            load_idx(0, 0)
            load_ids(0, 0, True)
            load_table(sp, 1)
            load_ids(0, 1, True)
            for t in range(1, TPB):
                load_idx(0, t)
            for r in range(2, NR):
                sp.wait_ge(low_made, HALVES * (r - 1))
                load_table(sp, r)
                load_ids(0, r, True)
                if r - 2 < TPB:
                    load_dense(0, r - 2)
            for dst, src in (
                (w1z[:], w1[P:P + NP, :].rearrange("(c p) n -> p c n", p=ZK)),
                (w1d[:], w1[0:P, :]), (w1_second, w1[P + NP:, :]),
                (w2s[:], w2.rearrange("(p c) n -> p c n", c=C1)),
                (w3s[:], w3.rearrange("(p c) one -> p (c one)", c=C2)),
                (b1s[:], b1.rearrange("(p c) -> p c", c=C1)),
                (b2s[:], b2.rearrange("(p c) -> p c", c=C2)),
            ):
                sp.dma_start(dst, src).then_inc(weights_loaded, 16)
            with sp.Fori(1, BLOCKS - 1) as b:
                load_block(b, "middle")
            load_block(BLOCKS - 1, "last")
            sp.wait_ge(stored, 16 * (BLOCKS + 1))

        @block.gpsimd
        def _(pool):
            def gather_block(b, share):
                for t in range(TPB):
                    pool.wait_ge(idx_loaded[t], 16 * (b + 1))
                    for k in range(T_FILLS):
                        if share != "first":
                            pool.wait_ge(transposed, NT * (b - 1) + T_FILLS * t + k + 1)
                            pool.sem_inc(rows_free, 1)
                        for f in in_fill(t, k, share):
                            if f > 0:
                                nc.gpsimd.indirect_dma_start(
                                    rows[:, t, SLOT[f], :], None, tables[f - 1],
                                    bass.IndirectOffsetOnAxis(ap=idx[:, t, f - 1:f], axis=0),
                                ).then_inc(gathered[t][k], 16)

            nc.gpsimd.iota(row_i32[:], pattern=[[1, V_C]], base=0, channel_multiplier=V_C).then_inc(numbers_made, 1)
            nc.gpsimd.memset(ident[:], 0.0).then_inc(ident_zeroed, 1)
            pool.wait_ge(ident_zeroed, 1)
            nc.gpsimd.affine_select(out=ident[:], in_=ident[:], compare_op=ALU.not_equal, fill=1.0,
                                    base=0, pattern=[[-1, P]], channel_multiplier=1).then_inc(ident_ready, 1)
            gather_block(0, "first")
            with pool.Fori(1, BLOCKS - 1) as b:
                gather_block(b, "middle")
            gather_block(BLOCKS - 1, "last")

        @block.tensor
        def _(pe):
            def transposes(b, t, k, share):
                n = T_FILLS * t + k
                if k == 0:
                    pe.wait_ge(dense_loaded[t], 16 * (b + 1))
                pe.wait_ge(gathered[t][k], 16 * gathers(b, t, k, share))
                if n >= 2 or share != "first":
                    pe.wait_ge(emb_by_s if n % 2 else emb_by_v, NT // 2 * b + n // 2)
                for i, f in enumerate(in_fill(t, k, share)):
                    last = nc.tensor.transpose(t_bank[n % 2][:, i * P:(i + 1) * P], rows[:, t, SLOT[f], :], ident[:])
                last.then_inc(transposed, 1)

            def products(b, t, k, share):
                m = G_FILLS * t + k
                if k == 0:
                    n = T_FILLS * (t + 1)
                    pe.wait_ge(emb_by_v, NT // 2 * b + n // 2)
                    pe.wait_ge(emb_by_s, NT // 2 * b + n // 2)
                    if t == 0:
                        pe.wait_ge(lookup_by_s, lookups(b, N_LOOKUPS[share], share == "first"))
                if not (share == "first" and m < 3):
                    ago = 3 if m + G_FILLS >= 3 else 2
                    pe.wait_ge(gram_by_v, NG * b + m - ago + 1)
                    pe.wait_ge(gram_by_s, NG * b + m - ago + 1)
                for i in range(GQ):
                    group = emb_t[:, t % TPB, J * (GQ * k + i):J * (GQ * k + i + 1), :]
                    last = nc.tensor.matmul(g_bank[(m + G_FILLS) % G_BANKS][0:GP, i * J * NF:(i + 1) * J * NF],
                                            group.rearrange("p j f -> p (j f)")[:, 0:GP], group[:, :, 0:NF],
                                            start=True, stop=True)
                last.then_inc(multiplied, 1)

            def select(b, o, h, share):
                first = share == "first"
                to, cols = lookup_bank(o, first), slice(P * FROM_TILE[share][o], COLS)
                if h == 0 and (not first or o > 1):
                    pe.wait_ge(lookup_by_s, lookups(b, o, first) - first)
                if first:
                    pe.wait_ge(low_made, HALVES * o + h + 1)
                pe.wait_ge(onehot_made, HALVES * lookups(b, o, first) + h + 1)
                for c in range(HC):
                    for i in range(3):
                        last = nc.tensor.matmul(to[:, cols], parts[o][:, i, HC * h + c, :], onehot[:, h, c, cols],
                                                start=(h == c == i == 0),
                                                stop=(h == HALVES - 1 and c == HC - 1 and i == 2))
                last.then_inc(looked_up if h == HALVES - 1 else onehot_used, 1)

            def dense_share(i, part, to):
                s0, count = groups(part)
                dense_cols = dense_t[:].rearrange("p (j s) -> p j s", j=J)[:, :, s0:s0 + count]
                nc.tensor.matmul(to[:, 0:J * count], w1d[:, i:H1:C1], dense_cols, start=True, stop=False)

            def unit(b, n, part):
                kind, i = UNITS[n]
                to, banks = unit_bank(n, part), unit_banks(part)
                done = rounds_done(b, part)
                s0, count = groups(part)
                n_cols = J * count
                if n == 0:
                    pe.wait_ge(unit_by_s, emptied_by("S", NU) * done + 1)
                if n >= len(banks):
                    last_fill = n - len(banks)
                    if UNIT_ENGINE[last_fill] == "V":
                        pe.wait_ge(unit_by_v, emptied_by("V", NU) * done + emptied_by("V", last_fill + 1))
                    else:
                        pe.wait_ge(unit_by_s, emptied_by("S", NU) * done + emptied_by("S", last_fill + 1) + 1)
                if kind == "rows":
                    if i == 0:
                        made = NG * b + (NG // 2 if part == 0 else 0)
                        pe.wait_ge(gram_by_v, made)
                        pe.wait_ge(gram_by_s, made)
                    for q, a in enumerate(range(TQ * i, min(TQ * i + TQ, NF - 1))):
                        last = nc.tensor.transpose(to[0:count, q * P:q * P + GP], gram[0:GP, s0:s0 + count, a],
                                                   ident[0:GP, 0:GP])
                elif kind == "pairs":
                    if i == 0:
                        pe.wait_ge(unit_by_v, emptied_by("V", NU) * done + emptied_by("V", ROWS_DONE))
                        pe.wait_ge(unit_by_s, emptied_by("S", NU) * done + emptied_by("S", ROWS_DONE) + 1)
                    for j in range(J):
                        last = nc.tensor.transpose(to[0:ZK, j * count:(j + 1) * count],
                                                   pair_rows[0:count, j, i * ZK:(i + 1) * ZK], ident[0:count, 0:count])
                elif kind == "layer1":
                    cols = slice(i, H1, C1)
                    if part != 1:
                        if i == 0:
                            pe.wait_ge(weights_loaded, 16 * N_WEIGHTS)
                            pe.wait_ge(w1d_ready, 1)
                            pe.wait_ge(dense_t_ready, done + 1)
                        dense_share(i, part, to)
                    if i == 0:
                        pe.wait_ge(unit_by_v, emptied_by("V", NU) * done + emptied_by("V", PAIRS_DONE))
                        pe.wait_ge(unit_by_s, emptied_by("S", NU) * done + emptied_by("S", PAIRS_DONE) + 1)
                    for c in range(ZC):
                        last = nc.tensor.matmul(to[:, 0:n_cols], w1z[:, c, cols], pair_cols[:, c, 0:n_cols],
                                                start=False, stop=(c == ZC - 1))
                elif kind == "layer2":
                    for c in range(C1):
                        if i == 0 and c in (0, C1 - 1):
                            pe.wait_ge(unit_by_s, emptied_by("S", NU) * done + emptied_by("S", L1_DONE) + (c > 0))
                        last = nc.tensor.matmul(to[:, 0:n_cols], w2s[:, c, i:H2:C2], h1[:, c, 0:n_cols],
                                                start=(c == 0), stop=(c == C1 - 1))
                elif part == 1:
                    for c in range(C2):
                        pe.wait_ge(unit_by_s, emptied_by("S", NU) * done + emptied_by("S", L2_DONE) - C2 + c + 2)
                        last = nc.tensor.matmul(to[0:1, 0:n_cols], w3s[:, c:c + 1], h2[:, c, 0:n_cols],
                                                start=(c == 0), stop=(c == C2 - 1))
                else:
                    pe.wait_ge(h2_weighted, done + 1)
                    last = nc.tensor.matmul(to[0:1, 0:n_cols], ones[:], h2[:, 0, 0:n_cols], start=True, stop=True)
                last.then_inc(unit_filled, 1)

            def body(b, plan):
                share = share_of(plan)
                first = share == "first"
                for kind, *at in plan:
                    if kind == "T":
                        transposes(b, *at, share)
                    elif kind == "G":
                        if first and at == [0, 0]:
                            pe.wait_ge(pad_zeroed, 1)
                        products(b, *at, share)
                    elif kind == "O":
                        select(b, *at, share)
                    elif kind == "P":
                        i, = at
                        if i == 0:
                            pe.wait_ge(dense_t_ready, b + 1)
                        dense_share(i, 1, EARLY_BANKS[i])
                    elif kind == "W":
                        unit(b, *at)

            pe.wait_ge(ident_ready, 1)
            for _ in range(CLOCK_STARTERS):
                nc.tensor.transpose(t_bank[0][:, 0:P], ident[:], ident[:])
            blocks(pe, body)

        def empty_tile_bank(eng, b, t, k, share):
            n = T_FILLS * t + k
            fs = in_fill(t, k, share)
            eng.wait_ge(transposed, NT * b + n + 1)
            src = t_bank[n % 2][:, 0:len(fs) * P].rearrange("p (f s) -> p s f", f=len(fs))
            return emb_t[:, t, :, fs[0]:fs[-1] + 1], src

        def gram_part(m, t, k, j):
            q = slice(32 * j, min(32 * j + 32, GP))
            src = g_bank[(m + G_FILLS) % G_BANKS][:, 0:GQ * J * NF].rearrange("p (g j b) -> p g j b", g=GQ, j=J)
            s = U * (t % TPB) + GQ * k
            return gram[q, s:s + GQ, :], src[q, :, j, :]

        def filled_bank(eng, b, n, part):
            eng.wait_ge(unit_filled, NU * rounds_done(b, part) + n + 1)
            return unit_bank(n, part)

        def empty_unit(copy, n, part, src):
            work, i = UNITS[n]
            s0, count = groups(part)
            if work == "pairs":
                return copy(pair_cols[:, i, 0:J * count], src[0:ZK, 0:J * count])
            for q, a in enumerate(range(TQ * i, min(TQ * i + TQ, NF - 1))):
                first_pair = a * NF - a * (a + 1) // 2
                block_a = src[0:count, q * P:(q + 1) * P].rearrange("p (j b) -> p j b", j=J)
                last = copy(pair_rows[0:count, :, first_pair:first_pair + NF - 1 - a], block_a[:, :, a + 1:NF])
            return last

        @block.vector
        def _(dve):
            def cut_rest(r, h):
                dve.wait_ge(high_made, HALVES * r + h + 1)
                if r > 0:
                    dve.wait_ge(low_made, HALVES * (r - 1) + h + 1)
                nc.vector.tensor_tensor(half(rest, h), half(table_in[r % 2], h), part(r, 0, h), ALU.subtract
                                        ).then_inc(rest_made, 1)

            def cut_low(r, h):
                dve.wait_ge(mid_made, HALVES * r + h + 1)
                nc.vector.tensor_tensor(part(r, 2, h), half(rest, h), part(r, 1, h), ALU.subtract
                                        ).then_inc(low_made, 1)

            def one_hot(b, o, h, share):
                first = share == "first"
                if h == 0:
                    dve.wait_ge(ids_turned, lookups(b, o, first) + 1)
                if not first or o > 0:
                    if h < HALVES - 1:
                        dve.wait_ge(onehot_used, lookups(b, o, first))
                    else:
                        dve.wait_ge(looked_up, lookups(b, o, first))
                cols = slice(P * FROM_TILE[share][o], COLS)
                for c in range(HC):
                    at = HC * h + c
                    last = nc.vector.tensor_scalar(onehot[:, h, c, cols], ids_f16[0:V_K, o % 2, cols],
                                                   row_f32[:, at:at + 1], None, ALU.is_equal)
                last.then_inc(onehot_made, 1)

            dve.wait_ge(numbers_made, 1)
            nc.vector.tensor_copy(row_f32[:], row_i32[:]).then_inc(row_ready, 1)
            nc.vector.memset(ones[:], 1.0)
            nc.vector.memset(emb_t[:, :, :, NF:], 0.0).then_inc(pad_zeroed, 1)
            dve.wait_ge(row_ready, 1)

            def body(b, plan):
                share = share_of(plan)
                first = share == "first"
                for kind, *at in plan:
                    if kind == "T":
                        t, k = at
                        if (T_FILLS * t + k) % 2 == 0:
                            if not first and t == k == 0:
                                dve.wait_ge(dense_t_ready, b)
                            dst, src = empty_tile_bank(dve, b, t, k, share)
                            nc.vector.tensor_copy(dst, src).then_inc(emb_by_v, 1)
                    elif kind == "G":
                        t, k = at
                        m = G_FILLS * t + k
                        dve.wait_ge(multiplied, NG * b + m + 1)
                        for j in (0, 1):
                            last = nc.vector.tensor_copy(*gram_part(m, t, k, j))
                        last.then_inc(gram_by_v, 1)
                    elif kind == "R":
                        cut_rest(*at)
                    elif kind == "M":
                        cut_low(*at)
                    elif kind == "H":
                        one_hot(b, *at, share)
                    elif kind == "A":
                        dve.wait_ge(weights_loaded, 16 * N_WEIGHTS)
                        nc.vector.tensor_tensor(w1d[:], w1d[:], w1_second, ALU.add).then_inc(w1d_ready, 1)
                        dve.wait_ge(w1d_ready, 1)
                    elif kind == "V":
                        done = rounds_done(b, at[0])
                        total = h2[:, 0, 0:J * groups(at[0])[1]]
                        for c in range(C2):
                            dve.wait_ge(unit_by_s, emptied_by("S", NU) * done + emptied_by("S", L2_DONE) - C2 + c + 2)
                            if c == 0:
                                nc.vector.tensor_scalar(total, total, w3s[:, 0:1], None, ALU.mult
                                                        ).then_inc(h2_scaled[0], 1)
                            else:
                                dve.wait_ge(h2_scaled[c - 1], done + 1)
                                nc.vector.scalar_tensor_tensor(
                                    out=total, in0=h2[:, c, 0:J * groups(at[0])[1]], scalar=w3s[:, c:c + 1], in1=total,
                                    op0=ALU.mult, op1=ALU.add
                                ).then_inc(h2_scaled[c] if c < C2 - 1 else h2_weighted, 1)
                    elif kind == "W" and UNIT_ENGINE[at[0]] == "V":
                        empty_unit(nc.vector.tensor_copy, *at, filled_bank(dve, b, *at)).then_inc(unit_by_v, 1)

            blocks(dve, body)

        @block.scalar
        def _(act):
            def cut_high(r, h):
                act.wait_ge(table_loaded[r % 2][h], 16 * (r // 2 + 1))
                nc.scalar.copy(part(r, 0, h), half(table_in[r % 2], h)).then_inc(high_made, 1)

            def cut_middle(r, h):
                act.wait_ge(rest_made, HALVES * r + h + 1)
                nc.scalar.copy(part(r, 1, h), half(rest, h)).then_inc(mid_made, 1)

            load_table(act, 0)

            def body(b, plan):
                share = share_of(plan)
                first = share == "first"
                for kind, *at in plan:
                    if kind == "T":
                        t, k = at
                        if (T_FILLS * t + k) % 2 == 1:
                            dst, src = empty_tile_bank(act, b, t, k, share)
                            nc.scalar.copy(dst, src).then_inc(emb_by_s, 1)
                    elif kind == "G":
                        t, k = at
                        m = G_FILLS * t + k
                        act.wait_ge(multiplied, NG * b + m + 1)
                        for j in (2, 3):
                            last = nc.scalar.copy(*gram_part(m, t, k, j))
                        last.then_inc(gram_by_s, 1)
                    elif kind == "I":
                        o, = at
                        act.wait_ge(ids_loaded[o % 2], 16 * slot_loads(b, o, first))
                        if not first or o >= 2:
                            act.wait_ge(onehot_made, HALVES * lookups(b, max(o - 1, 0), first))
                        nc.scalar.copy(ids_f16[:, o % 2, :], ids_row[:, o % 2, :]).then_inc(ids_turned, 1)
                    elif kind == "R":
                        cut_high(*at)
                    elif kind == "M":
                        cut_middle(*at)
                    elif kind == "O" and at[1] == HALVES - 1:
                        o = at[0]
                        act.wait_ge(looked_up, lookups(b, o, first) + 1)
                        t = FROM_TILE[share][o]
                        nc.scalar.copy(emb_t[:, t:, :, RESIDENT[o] + 1],
                                       lookup_bank(o, first)[:, P * t:].rearrange("p (t s) -> p t s", t=TPB - t)
                                       ).then_inc(lookup_by_s, 1)
                    elif kind == "D":
                        part, = at
                        if not first and part != 1:
                            act.wait_ge(stored, 16 * b)
                            act.wait_ge(unit_filled, NU * (b - 1) + L1_DONE)
                        tiles = {None: range(TPB), 0: range(TPB // 2), 1: range(TPB // 2, TPB)}[part]
                        act.wait_ge(emb_by_v, NT // 2 * b + T_FILLS // 2 * tiles[-1] + 1)
                        for t in tiles:
                            last = nc.scalar.copy(
                                dense_t[:].rearrange("p (j t u) -> p t j u", j=J, t=TPB)[:, t],
                                emb_t[:, t, :, 0].rearrange("p (u j) -> p j u", j=J))
                        last.then_inc(dense_t_ready, 1)
                    elif kind == "A":
                        act.wait_ge(weights_loaded, 16 * N_WEIGHTS)
                        nc.scalar.copy(y[:, 0:1], b1s[0:1, 0:1]).then_inc(unit_by_s, 1)
                    elif kind == "W" and UNIT_ENGINE[at[0]] == "S":
                        n, part = at
                        work, i = UNITS[n]
                        src = filled_bank(act, b, n, part)
                        done = rounds_done(b, part)
                        n_cols = J * groups(part)[1]
                        if work == "layer1":
                            last = nc.scalar.activation(h1[:, i, 0:n_cols], src[:, 0:n_cols], ACT.Relu, bias=b1s[:, i:i + 1])
                        elif work == "layer2":
                            last = nc.scalar.activation(h2[:, i, 0:n_cols], src[:, 0:n_cols], ACT.Relu, bias=b2s[:, i:i + 1])
                        elif work != "layer3":
                            last = empty_unit(nc.scalar.copy, n, part, src)
                        else:
                            if part == 1:
                                act.wait_ge(stored, 16 * done)
                            tiles = TPB if part is None else TPB // 2
                            last = nc.scalar.copy(y[:, 0:n_cols].rearrange("o (u j t) -> o j t u", j=J, t=tiles),
                                                  src[0:1, 0:n_cols].rearrange("o (j t u) -> o j t u", j=J, t=tiles))
                        last.then_inc(unit_by_s, 1)
                        if work == "layer3":
                            act.wait_ge(unit_by_s, emptied_by("S", NU) * (done + 1) + 1)
                            start = TPB * (b - 1) if part is None else TPB * (BLOCKS - 1) + part * tiles
                            act.dma_start(out_tiles[:, bass.ds(start, tiles)],
                                          y[:, 0:n_cols].rearrange("o (q t) -> o q t", t=tiles)).then_inc(stored, 16)

            blocks(act, body)


N_TABLES = 26
_INS = ["r_dense_features", "ids"] + [f"tbl_{i}" for i in range(N_TABLES)] + ["W_top1", "b_top1", "W_top2", "b_top2", "W_top3"]


def kernel(**inputs):
    import numpy as _np
    import concourse.bacc as _bacc
    from concourse import mybir as _mybir
    from concourse.bass_utils import run_bass_kernel_spmd as _run

    nc = _bacc.Bacc("TRN2", target_bir_lowering=False, num_devices=1)
    arrays, aps = {}, {}
    for name in _INS:
        a = _np.ascontiguousarray(inputs[name])
        arrays[f"in_{name}"] = a
        aps[name] = nc.dram_tensor(f"in_{name}", a.shape, _mybir.dt.from_np(a.dtype), kind="ExternalInput").ap()
    batch, n_tab = arrays["in_ids"].shape
    a = _np.ascontiguousarray(arrays["in_ids"].reshape(P, batch // P, n_tab).transpose(2, 1, 0).reshape(n_tab, batch))
    arrays["in_ids_t"] = a
    ids_t = nc.dram_tensor("in_ids_t", a.shape, _mybir.dt.from_np(a.dtype), kind="ExternalInput").ap()
    out = nc.dram_tensor("out_y", (batch, 1), F32, kind="ExternalOutput").ap()
    dlrm_tower(nc, aps["r_dense_features"], aps["ids"], ids_t, [aps[f"tbl_{i}"] for i in range(N_TABLES)],
               aps["W_top1"], aps["b_top1"], aps["W_top2"], aps["b_top2"], aps["W_top3"], out)
    r = _run(nc, [arrays], core_ids=[0])
    return r.results[0]["out_y"]
```
